# Optimizing a Trainium2 kernel written in Bass

```python
import numpy as np
import jax
import jax.numpy as jnp

def _softmax(x, axis=-1):
    return jax.nn.softmax(x, axis=axis)

def _gelu(x):
    return jax.nn.gelu(x, approximate=True)

def _silu(x):
    return jax.nn.silu(x)

def _sigmoid(x):
    return jax.nn.sigmoid(x)

def _layernorm(x, axis=-1, eps=1e-05):
    m = jnp.mean(x, axis=axis, keepdims=True)
    v = jnp.var(x, axis=axis, keepdims=True)
    return (x - m) / jnp.sqrt(v + eps)

def _scatter_add(tgt, idx, src, axis=0):
    return tgt.at[idx].add(src)

def _segment_sum(src, seg, n):
    return jax.ops.segment_sum(src, seg, n)
kernel_name = 'mk_dlrm_tower_d1_rec_r8_57714a'

def setup_inputs(seed: int=0):
    np.random.seed(seed)
    _w = jnp.asarray

    def _rec_inputs():
        import jax
        import jax.numpy as jnp
        _tk = jax.random.key(seed)
        ids = jnp.stack([jax.random.randint(jax.random.fold_in(_tk, 200 + f), (2048,), 0, v, jnp.int32) for f, v in enumerate([1000, 1250, 1250, 1250, 1000, 1250, 12500, 125000, 1000, 12500, 1000, 1250, 1000, 1250, 1250, 1250, 1000, 1000, 12500, 12500, 1250, 1000, 1000, 12500, 1000, 12500])], axis=1)
        tbl_0 = 0.05 * jax.random.normal(jax.random.fold_in(_tk, 500 + 0), (1000, 128), jnp.float32)
        tbl_1 = 0.05 * jax.random.normal(jax.random.fold_in(_tk, 500 + 1), (1250, 128), jnp.float32)
        tbl_2 = 0.05 * jax.random.normal(jax.random.fold_in(_tk, 500 + 2), (1250, 128), jnp.float32)
        tbl_3 = 0.05 * jax.random.normal(jax.random.fold_in(_tk, 500 + 3), (1250, 128), jnp.float32)
        tbl_4 = 0.05 * jax.random.normal(jax.random.fold_in(_tk, 500 + 4), (1000, 128), jnp.float32)
        tbl_5 = 0.05 * jax.random.normal(jax.random.fold_in(_tk, 500 + 5), (1250, 128), jnp.float32)
        tbl_6 = 0.05 * jax.random.normal(jax.random.fold_in(_tk, 500 + 6), (12500, 128), jnp.float32)
        tbl_7 = 0.05 * jax.random.normal(jax.random.fold_in(_tk, 500 + 7), (125000, 128), jnp.float32)
        tbl_8 = 0.05 * jax.random.normal(jax.random.fold_in(_tk, 500 + 8), (1000, 128), jnp.float32)
        tbl_9 = 0.05 * jax.random.normal(jax.random.fold_in(_tk, 500 + 9), (12500, 128), jnp.float32)
        tbl_10 = 0.05 * jax.random.normal(jax.random.fold_in(_tk, 500 + 10), (1000, 128), jnp.float32)
        tbl_11 = 0.05 * jax.random.normal(jax.random.fold_in(_tk, 500 + 11), (1250, 128), jnp.float32)
        tbl_12 = 0.05 * jax.random.normal(jax.random.fold_in(_tk, 500 + 12), (1000, 128), jnp.float32)
        tbl_13 = 0.05 * jax.random.normal(jax.random.fold_in(_tk, 500 + 13), (1250, 128), jnp.float32)
        tbl_14 = 0.05 * jax.random.normal(jax.random.fold_in(_tk, 500 + 14), (1250, 128), jnp.float32)
        tbl_15 = 0.05 * jax.random.normal(jax.random.fold_in(_tk, 500 + 15), (1250, 128), jnp.float32)
        tbl_16 = 0.05 * jax.random.normal(jax.random.fold_in(_tk, 500 + 16), (1000, 128), jnp.float32)
        tbl_17 = 0.05 * jax.random.normal(jax.random.fold_in(_tk, 500 + 17), (1000, 128), jnp.float32)
        tbl_18 = 0.05 * jax.random.normal(jax.random.fold_in(_tk, 500 + 18), (12500, 128), jnp.float32)
        tbl_19 = 0.05 * jax.random.normal(jax.random.fold_in(_tk, 500 + 19), (12500, 128), jnp.float32)
        tbl_20 = 0.05 * jax.random.normal(jax.random.fold_in(_tk, 500 + 20), (1250, 128), jnp.float32)
        tbl_21 = 0.05 * jax.random.normal(jax.random.fold_in(_tk, 500 + 21), (1000, 128), jnp.float32)
        tbl_22 = 0.05 * jax.random.normal(jax.random.fold_in(_tk, 500 + 22), (1000, 128), jnp.float32)
        tbl_23 = 0.05 * jax.random.normal(jax.random.fold_in(_tk, 500 + 23), (12500, 128), jnp.float32)
        tbl_24 = 0.05 * jax.random.normal(jax.random.fold_in(_tk, 500 + 24), (1000, 128), jnp.float32)
        tbl_25 = 0.05 * jax.random.normal(jax.random.fold_in(_tk, 500 + 25), (12500, 128), jnp.float32)
        _rk = jax.random.fold_in(_tk, 7)
        r_dense_features = -0.000520686 + 1.00062 * jax.random.normal(jax.random.fold_in(_rk, 101), (2048, 128), jnp.float32)
        W_top1 = 0.0405887 * jax.random.normal(jax.random.fold_in(_tk, 801), (607, 512), jnp.float32)
        W_top2 = 0.0441942 * jax.random.normal(jax.random.fold_in(_tk, 802), (512, 256), jnp.float32)
        W_top3 = 0.0625 * jax.random.normal(jax.random.fold_in(_tk, 803), (256, 1), jnp.float32)
        b_top1 = jnp.zeros((512,), jnp.float32)
        b_top2 = jnp.zeros((256,), jnp.float32)
        return (r_dense_features, ids, tbl_0, tbl_1, tbl_2, tbl_3, tbl_4, tbl_5, tbl_6, tbl_7, tbl_8, tbl_9, tbl_10, tbl_11, tbl_12, tbl_13, tbl_14, tbl_15, tbl_16, tbl_17, tbl_18, tbl_19, tbl_20, tbl_21, tbl_22, tbl_23, tbl_24, tbl_25, W_top1, b_top1, W_top2, b_top2, W_top3)
    r_dense_features, ids, tbl_0, tbl_1, tbl_2, tbl_3, tbl_4, tbl_5, tbl_6, tbl_7, tbl_8, tbl_9, tbl_10, tbl_11, tbl_12, tbl_13, tbl_14, tbl_15, tbl_16, tbl_17, tbl_18, tbl_19, tbl_20, tbl_21, tbl_22, tbl_23, tbl_24, tbl_25, W_top1, b_top1, W_top2, b_top2, W_top3 = _rec_inputs()

    def _L0_rec_setup():
        import jax, jax.numpy as jnp
        import numpy as np
        B, F, D = (2048, 26, 128)
        key = jax.random.key(seed)
        k1, k2 = jax.random.split(key)
        dense_features = jax.random.normal(k1, (B, D), dtype=jnp.float32)
        sparse_values = jax.random.normal(k2, (B, F, D), dtype=jnp.float32)
        return {'dense_features': dense_features, 'sparse_values': sparse_values}
    _L0_rec_all = _L0_rec_setup()
    _L0_rec_in = {k: v for k, v in _L0_rec_all.items() if k in ()}
    del _L0_rec_all
    return {'r_dense_features': r_dense_features, 'ids': ids, 'tbl_0': tbl_0, 'tbl_1': tbl_1, 'tbl_2': tbl_2, 'tbl_3': tbl_3, 'tbl_4': tbl_4, 'tbl_5': tbl_5, 'tbl_6': tbl_6, 'tbl_7': tbl_7, 'tbl_8': tbl_8, 'tbl_9': tbl_9, 'tbl_10': tbl_10, 'tbl_11': tbl_11, 'tbl_12': tbl_12, 'tbl_13': tbl_13, 'tbl_14': tbl_14, 'tbl_15': tbl_15, 'tbl_16': tbl_16, 'tbl_17': tbl_17, 'tbl_18': tbl_18, 'tbl_19': tbl_19, 'tbl_20': tbl_20, 'tbl_21': tbl_21, 'tbl_22': tbl_22, 'tbl_23': tbl_23, 'tbl_24': tbl_24, 'tbl_25': tbl_25, 'W_top1': W_top1, 'b_top1': b_top1, 'W_top2': W_top2, 'b_top2': b_top2, 'W_top3': W_top3}

def reference(r_dense_features, ids, tbl_0, tbl_1, tbl_2, tbl_3, tbl_4, tbl_5, tbl_6, tbl_7, tbl_8, tbl_9, tbl_10, tbl_11, tbl_12, tbl_13, tbl_14, tbl_15, tbl_16, tbl_17, tbl_18, tbl_19, tbl_20, tbl_21, tbl_22, tbl_23, tbl_24, tbl_25, W_top1, b_top1, W_top2, b_top2, W_top3):
    import jax
    import jax.numpy as jnp

    def _L0_rec_ref(dense_features, sparse_values):
        import jax, jax.numpy as jnp
        import numpy as np
        B, F, D = (2048, 26, 128)
        sd = jnp.einsum('bfd,bd->bf', sparse_values, dense_features)
        ss = jnp.einsum('bfd,bgd->bfg', sparse_values, sparse_values)
        iu, ju = jnp.triu_indices(F, k=1)
        pairs = ss[:, iu, ju]
        return jnp.concatenate([dense_features, sd, pairs], axis=1)
    e = jnp.stack([tbl_0[ids[:, 0]], tbl_1[ids[:, 1]], tbl_2[ids[:, 2]], tbl_3[ids[:, 3]], tbl_4[ids[:, 4]], tbl_5[ids[:, 5]], tbl_6[ids[:, 6]], tbl_7[ids[:, 7]], tbl_8[ids[:, 8]], tbl_9[ids[:, 9]], tbl_10[ids[:, 10]], tbl_11[ids[:, 11]], tbl_12[ids[:, 12]], tbl_13[ids[:, 13]], tbl_14[ids[:, 14]], tbl_15[ids[:, 15]], tbl_16[ids[:, 16]], tbl_17[ids[:, 17]], tbl_18[ids[:, 18]], tbl_19[ids[:, 19]], tbl_20[ids[:, 20]], tbl_21[ids[:, 21]], tbl_22[ids[:, 22]], tbl_23[ids[:, 23]], tbl_24[ids[:, 24]], tbl_25[ids[:, 25]]], axis=1)
    z = _L0_rec_ref(r_dense_features, e)
    z = z.reshape(z.shape[0], -1)
    h = jnp.concatenate([z, r_dense_features], axis=1)
    h = jnp.maximum(h @ W_top1 + b_top1, 0.0)
    h = jnp.maximum(h @ W_top2 + b_top2, 0.0)
    y = h @ W_top3
    return y

_drawn_inputs = setup_inputs


def setup_inputs(seed=0):
    import zlib

    import numpy as np

    out = dict(_drawn_inputs(seed))
    spreads = {'b_top1': (0.0, 0.1), 'b_top2': (0.0, 0.1)}
    factors = {}
    for name, (base, spread) in spreads.items():
        noise = np.random.default_rng([zlib.crc32(name.encode()), seed]).standard_normal(out[name].shape)
        drawn = base * np.exp(spread * noise) if base else spread * noise
        out[name] = jnp.asarray(drawn.astype(out[name].dtype))
    for name, factor in factors.items():
        out[name] = (out[name] * factor).astype(out[name].dtype)
    return out
```

```python
from contextlib import ExitStack

import numpy as np

import concourse.bass as bass
from concourse import mybir

P = 128
BATCH = 2048
D = 128
FIELDS = 26
FEATURES = FIELDS + 1
TILE = 256
TILES = BATCH // TILE
SUBS = TILE // P
H1, H2 = 512, 256

ONE_HOT = [0, 4, 8, 10, 12, 16]
GATHERED = [f for f in range(FIELDS) if f not in ONE_HOT]
OH = len(ONE_HOT)
OH_ROWS = 1000
CHUNKS = 8
OH_P = OH_ROWS // CHUNKS
PARTS = 3

GATHERS = len(GATHERED)
WEIGHT_LOADS = 9
GROUP = 4
GROUPS = len(GATHERED) // GROUP
assert GROUPS * GROUP == len(GATHERED)
TURNS = SUBS * GROUPS
TURN_SLOTS = 4
BANK = 512

FPAD = 32
QUAD = 4
COLS = FEATURES - 1
QUADS = TILE // QUAD
PER = 8
GRAMS = QUADS // PER

ORDER = [0] + [1 + f for f in ONE_HOT] + [1 + f for f in GATHERED]
PAIRS = FEATURES * COLS // 2
PAIR_CHUNKS = -(-PAIRS // P)


def pair_start(i):
    return i * COLS - i * (i - 1) // 2


def weight_rows():
    rows = []
    for i in range(FEATURES):
        for j in range(i + 1, FEATURES):
            a, b = sorted((ORDER[i], ORDER[j]))
            rows.append(D + pair_start(a) + b - a - 1)
    return rows + list(range(D)) + list(range(D + PAIRS, 2 * D + PAIRS))


def row_moves():
    moves = []
    for i in range(COLS):
        j, n = i + 1, COLS - i
        while n:
            at = pair_start(i) + j - i - 1
            k = min(n, P - at % P)
            moves.append((i, j, k, at // P, at % P))
            j, n = j + k, n - k
    return moves


MOVES = row_moves()

F32 = mybir.dt.float32
BF16 = mybir.dt.bfloat16
F16 = mybir.dt.float16
I32 = mybir.dt.int32
ALU = mybir.AluOpType
ACT = mybir.ActivationFunctionType

L1_BLOCKS = H1 // P
L2_BLOCKS = H2 // P
MLP_USES = L1_BLOCKS + L2_BLOCKS + 1


def build(nc, x_t, ids_gather, ids_one_hot, tables, w1, b1, w2, b2, w3, out):
    with ExitStack() as ctx:
        def sb(name, shape, dt=F32):
            return ctx.enter_context(nc.sbuf_tensor(name, shape, dt))

        def psum(name, shape):
            return ctx.enter_context(nc.psum_tensor(name, shape, F32))

        def sem(name):
            return ctx.enter_context(nc.semaphore(name))

        ident = sb("ident", [P, P])
        select = sb("select", [P, OH, P], F16)
        row_i = sb("row_i", [P, CHUNKS], I32)
        row_f = sb("row_f", [P, CHUNKS])
        table_parts = sb("table_parts", [P, PARTS, OH, CHUNKS, D], BF16)
        idx = [sb(f"idx{b}", [P, SUBS, GATHERS], I32) for b in range(2)]
        oh_ids = sb("oh_ids", [OH, BATCH], I32)
        oh_ids_h = sb("oh_ids_h", [P, BATCH], F16)
        one_hot = sb("one_hot", [P, 2, CHUNKS, TILE], BF16)
        x_sb = sb("x_sb", [P, BATCH])
        rows = sb("rows", [P, 2, SUBS, GATHERS, D])
        ET = sb("ET", [P, QUADS, QUAD, FPAD])
        gram = sb("gram", [P, COLS, TILE])
        z = [sb(f"z{b}", [P, PAIR_CHUNKS, TILE]) for b in range(2)]
        w1_sb = sb("w1_sb", [P, PAIR_CHUNKS + 1, H1])
        w1_again = sb("w1_again", [P, H1])
        w2_sb = sb("w2_sb", [P, L1_BLOCKS, H2])
        w3_sb = sb("w3_sb", [P, L2_BLOCKS])
        b1_sb = sb("b1_sb", [P, L1_BLOCKS])
        b2_sb = sb("b2_sb", [P, L2_BLOCKS])
        h1 = sb("h1", [P, L1_BLOCKS, TILE])
        h2 = sb("h2", [P, L2_BLOCKS, TILE])
        y = sb("y", [1, BATCH])
        table_f32 = gram[:, :, :].rearrange("p j b -> p (j b)")[:, 0:OH * CHUNKS * D]
        table_f32 = table_f32.rearrange("p (t c d) -> p t c d", t=OH, c=CHUNKS)

        ps_blocks = psum("ps_blocks", [P, TURN_SLOTS * GROUP, P])
        ps_turn = ps_blocks[:, :, :].rearrange("p (slot k) b -> p slot k b", k=GROUP)
        ps_gram = ps_blocks[:, :, :].rearrange("p (slot q) c -> p slot q c", q=PER)
        ps_ids = psum("ps_ids", [P, 2, BANK])
        ps_acc = psum("ps_acc", [P, 2, BANK])

        idx_in = [sem(f"idx_in{b}") for b in range(2)]
        oh_ids_in = sem("oh_ids_in")
        x_in = sem("x_in")
        rows_in = [[[sem(f"rows_in{b}_{s}_{g}") for g in range(GROUPS)] for s in range(SUBS)] for b in range(2)]
        w_in = sem("w_in")
        table_in = [sem(f"table_in{t}") for t in range(OH)]
        zeroed = sem("zeroed")
        consts = sem("consts")
        row_f_done = sem("row_f_done")
        ids_zero = sem("ids_zero")
        ids_cast = sem("ids_cast")
        part_hi = sem("part_hi")
        rest_1 = sem("rest_1")
        part_mid = sem("part_mid")
        part_lo = sem("part_lo")
        w1_summed = sem("w1_summed")
        ids_spread = sem("ids_spread")
        one_hot_done = sem("one_hot_done")
        look_done = sem("look_done")
        look_out = sem("look_out")
        turned = [sem(f"turned{b}") for b in range(2)]
        turn_out = sem("turn_out")
        x_out = sem("x_out")
        gram_done = sem("gram_done")
        gram_out_dve = sem("gram_out_dve")
        gram_out_act = sem("gram_out_act")
        z_in = sem("z_in")
        acc_done = sem("acc_done")
        acc_out = sem("acc_out")
        z_read = [sem(f"z_read{b}") for b in range(2)]
        y_out = sem("y_out")

        def static(i, *tiles):
            return isinstance(i, int) and i in tiles

        def gram_block(g, s):
            at = s * QUADS + g * PER
            return (gram[0:COLS, :, at:at + PER],
                    ps_gram[s * FPAD:s * FPAD + COLS, g % 2, :, s * COLS:(s + 1) * COLS].rearrange("i q j -> i j q"))

        block = ctx.enter_context(nc.Block())

        @block.sync
        def _(sp):
            def load_idx(first, b):
                sp.dma_start(idx[b][:, :, :], ids_gather[bass.ds(first, TILE), :].rearrange(
                    "(s p) f -> p s f", p=P)).then_inc(idx_in[b], 16)

            def next_idx(i, u, b):
                first = sp.snap((i + 2) * TILE)
                sp.wait_ge(turned[b], TURNS * (u + 1))
                load_idx(first, b)

            def move_pairs(i, u, b, first=False):
                copies = sp.snap(2 * GRAMS * (i + 1))
                sp.wait_ge(gram_out_act, copies)
                sp.wait_ge(gram_out_dve, copies)
                if not first:
                    sp.wait_ge(z_read[b], u)
                for row, j, k, c, p in MOVES:
                    sp.dma_start(z[b][p:p + k, c, :], gram[row:row + 1, j - 1:j - 1 + k, :]).then_inc(z_in, 16)

            load_idx(0, 0)
            load_idx(TILE, 1)
            sp.dma_start(oh_ids[:, :], ids_one_hot).then_inc(oh_ids_in, 16)
            for t in range(OH):
                sp.dma_start(table_f32[0:OH_P, t, :, :], tables[ONE_HOT[t]].rearrange(
                    "(p c) d -> p c d", c=CHUNKS)).then_inc(table_in[t], 16)
            sp.dma_start(x_sb[:, :], x_t).then_inc(x_in, 16)
            for c in range(PAIR_CHUNKS):
                k = min(P, PAIRS - c * P)
                sp.dma_start(w1_sb[0:k, c, :], w1[c * P:c * P + k, :]).then_inc(w_in, 16)
            sp.dma_start(w1_sb[:, PAIR_CHUNKS, :], w1[PAIRS:PAIRS + D, :]).then_inc(w_in, 16)
            sp.dma_start(w1_again[:, :], w1[PAIRS + D:PAIRS + 2 * D, :]).then_inc(w_in, 16)
            sp.dma_start(w2_sb[:, :, :], w2.rearrange("(c p) n -> p c n", p=P)).then_inc(w_in, 16)
            sp.dma_start(w3_sb[:, :], w3).then_inc(w_in, 16)
            sp.dma_start(b1_sb[:, :], b1).then_inc(w_in, 16)
            sp.dma_start(b2_sb[:, :], b2).then_inc(w_in, 16)

            for b in range(2):
                next_idx(b, 0, b)
                move_pairs(b, 0, b, first=True)
            with sp.Fori(1, TILES // 2 - 1) as u:
                for b in range(2):
                    next_idx(2 * u + b, u, b)
                    move_pairs(2 * u + b, u, b)
            for b in range(2):
                move_pairs(TILES - 2 + b, TILES // 2 - 1, b)

        @block.gpsimd
        def _(pool):
            pool.memset(ident[:, :], 0.0).then_inc(zeroed, 1)
            pool.memset(select[:, :, :], 0.0).then_inc(zeroed, 1)
            pool.memset(ET[:, :, :, FEATURES:FPAD], 0.0).then_inc(consts, 1)
            pool.iota(row_i[:, :], pattern=[[1, CHUNKS]], base=0, channel_multiplier=CHUNKS).then_inc(consts, 1)
            pool.wait_ge(zeroed, 2)
            pool.affine_select(out=ident[:, :], in_=ident[:, :], compare_op=ALU.not_equal, fill=1.0, base=0,
                               pattern=[[-1, P]], channel_multiplier=1).then_inc(consts, 1)
            pool.affine_select(out=select[:, :, :], in_=select[:, :, :], compare_op=ALU.not_equal, fill=1.0,
                               base=0, pattern=[[-1, OH], [0, P]], channel_multiplier=1).then_inc(consts, 1)

            def gather(b):
                for s in range(SUBS):
                    for n, f in enumerate(GATHERED):
                        pool.indirect_dma_start(
                            out=rows[:, b, s, n, :], out_offset=None, in_=tables[f],
                            in_offset=bass.IndirectOffsetOnAxis(ap=idx[b][:, s, n:n + 1], axis=0),
                        ).then_inc(rows_in[b][s][n // GROUP], 16)

            for b in range(2):
                pool.wait_ge(idx_in[b], 16)
                gather(b)
            landed = [pool.alloc_register(f"landed{b}") for b in range(2)]
            for b in range(2):
                pool.reg_mov(landed[b], 32)
            with pool.Fori(1, TILES // 2) as u:
                for b in range(2):
                    count = pool.snap(landed[b])
                    pool.wait_ge(turned[b], TURNS * u)
                    pool.wait_ge(idx_in[b], count)
                    pool.reg_add(landed[b], landed[b], 16)
                    gather(b)

        @block.vector
        def _(dve):
            dve.memset(oh_ids_h[:, :], 0.0).then_inc(ids_zero, 1)
            dve.wait_ge(consts, 4)
            dve.tensor_copy(row_f[:, :], row_i[:, :]).then_inc(row_f_done, 1)
            dve.wait_ge(oh_ids_in, 16)
            dve.wait_ge(ids_zero, 1)
            dve.tensor_copy(oh_ids_h[0:OH, :], oh_ids[:, :]).then_inc(ids_cast, 1)
            for t in range(OH):
                dve.wait_ge(part_hi, t + 1)
                dve.tensor_tensor(table_f32[0:OH_P, t, :, :], table_f32[0:OH_P, t, :, :],
                                  table_parts[0:OH_P, 0, t, :, :], ALU.subtract).then_inc(rest_1, 1)
                dve.wait_ge(part_mid, t + 1)
                dve.tensor_tensor(table_parts[0:OH_P, 2, t, :, :], table_f32[0:OH_P, t, :, :],
                                  table_parts[0:OH_P, 1, t, :, :], ALU.subtract).then_inc(part_lo, 1)
            dve.wait_ge(w_in, 16 * WEIGHT_LOADS)
            dve.tensor_tensor(w1_sb[:, PAIR_CHUNKS, :], w1_sb[:, PAIR_CHUNKS, :], w1_again[:, :],
                              ALU.add).then_inc(w1_summed, 1)
            dve.wait_ge(row_f_done, 1)

            def one_hots(i, first=False):
                for t in range(OH):
                    dve.wait_ge(ids_spread, OH * i + t + 1)
                    if t >= 2:
                        dve.wait_ge(look_done, OH * i + t - 1)
                    elif not first:
                        dve.wait_ge(look_done, OH * i)
                    dve.tensor_tensor(
                        one_hot[0:OH_P, t % 2, :, :],
                        ps_ids[0:OH_P, t % 2, 0:TILE].unsqueeze(1).to_broadcast([OH_P, CHUNKS, TILE]),
                        row_f[0:OH_P, :].unsqueeze(2).to_broadcast([OH_P, CHUNKS, TILE]),
                        ALU.is_equal).then_inc(one_hot_done, 1)

            def gram_out(i, first=False):
                if not first:
                    dve.wait_ge(z_in, 16 * len(MOVES) * i)
                for g in range(GRAMS):
                    dve.wait_ge(gram_done, GRAMS * i + g + 1)
                    for s in (0, 1):
                        dve.tensor_copy(*gram_block(g, s)).then_inc(gram_out_dve, 1)

            one_hots(0, first=True)
            gram_out(0, first=True)
            with dve.Fori(1, TILES) as i:
                one_hots(i)
                gram_out(i)

        @block.scalar
        def _(act):
            for t in range(OH):
                act.wait_ge(table_in[t], 16)
                act.activation(table_parts[0:OH_P, 0, t, :, :], table_f32[0:OH_P, t, :, :], ACT.Copy).then_inc(part_hi, 1)
                act.wait_ge(rest_1, t + 1)
                act.activation(table_parts[0:OH_P, 1, t, :, :], table_f32[0:OH_P, t, :, :], ACT.Copy).then_inc(part_mid, 1)
            act.wait_ge(x_in, 16)
            act.wait_ge(w_in, 16 * WEIGHT_LOADS)
            act.wait_ge(part_lo, OH)

            def features(i, first):
                if not first:
                    act.wait_ge(gram_done, GRAMS * i)
                act.activation(ET[:, :, :, 0].rearrange("d q s -> d s q"), x_sb[:, bass.ds(i * TILE, TILE)].rearrange(
                    "d (s q) -> d s q", s=QUAD), ACT.Copy).then_inc(x_out, 1)
                for t in range(OH):
                    act.wait_ge(look_done, OH * i + t + 1)
                    act.activation(ET[:, :, :, 1 + t].rearrange("d q s -> d s q"),
                                   ps_acc[:, t % 2, 0:TILE].rearrange("d (s q) -> d s q", s=QUAD), ACT.Copy).then_inc(look_out, 1)

            def copy_turned(i, u, b):
                for s in range(SUBS):
                    for g in range(GROUPS):
                        n = s * GROUPS + g
                        act.wait_ge(turned[b], TURNS * u + n + 1)
                        f = 1 + OH + g * GROUP
                        part = slice(s * QUAD // SUBS, (s + 1) * QUAD // SUBS)
                        act.activation(ET[:, :, part, f:f + GROUP].rearrange("d q s f -> d f s q"),
                                       ps_turn[:, n % TURN_SLOTS, :, :].rearrange("d f (s q) -> d f s q", q=QUADS), ACT.Copy).then_inc(turn_out, 1)

            def gram_out(i, first):
                if not first:
                    act.wait_ge(z_in, 16 * len(MOVES) * i)
                for g in range(GRAMS):
                    act.wait_ge(gram_done, GRAMS * i + g + 1)
                    for s in (2, 3):
                        act.activation(*gram_block(g, s), ACT.Copy).then_inc(gram_out_act, 1)

            def mlp_out(i):
                for m in range(L1_BLOCKS):
                    act.wait_ge(acc_done, MLP_USES * i + m + 1)
                    act.activation(h1[:, m, :], ps_acc[:, m % 2, 0:TILE], ACT.Relu,
                                   bias=b1_sb[:, m:m + 1]).then_inc(acc_out, 1)
                for m in range(L2_BLOCKS):
                    act.wait_ge(acc_done, MLP_USES * i + L1_BLOCKS + m + 1)
                    act.activation(h2[:, m, :], ps_acc[:, (L1_BLOCKS + m) % 2, 0:TILE], ACT.Relu,
                                   bias=b2_sb[:, m:m + 1]).then_inc(acc_out, 1)
                act.wait_ge(acc_done, MLP_USES * (i + 1))
                act.activation(y[:, bass.ds(i * TILE, TILE)], ps_acc[0:1, (MLP_USES - 1) % 2, 0:TILE],
                               ACT.Copy).then_inc(acc_out, 1)

            def tile(i, u, b):
                first = static(i, 0)
                features(i, first)
                copy_turned(i, u, b)
                gram_out(i, first)
                if not first:
                    mlp_out(i - 1)

            for b in range(2):
                tile(b, 0, b)
            with act.Fori(1, TILES // 2) as u:
                for b in range(2):
                    tile(2 * u + b, u, b)
            mlp_out(TILES - 1)
            act.wait_ge(acc_out, MLP_USES * TILES)
            act.dma_start(out.rearrange("b o -> o b"), y[:, :]).then_inc(y_out, 16)
            act.wait_ge(y_out, 16)

        @block.tensor
        def _(pe):
            def spread_ids(i, t):
                pe.matmul(ps_ids[0:OH_P, t % 2, 0:TILE], select[:, t, 0:OH_P], oh_ids_h[:, bass.ds(i * TILE, TILE)],
                          start=True, stop=True).then_inc(ids_spread, 1)

            def look_up(i):
                if not static(i, 0):
                    pe.wait_ge(one_hot_done, OH * i)
                spread_ids(i, 0)
                spread_ids(i, 1)
                for t in range(OH):
                    pe.wait_ge(one_hot_done, OH * i + t + 1)
                    if t >= 2:
                        pe.wait_ge(look_out, OH * i + t - 1)
                    elif not static(i, 0, 1):
                        pe.wait_ge(acc_out, MLP_USES * (i - 1))
                    elif i == 1:
                        pe.wait_ge(look_out, OH)
                    for c in range(CHUNKS):
                        for part in range(PARTS):
                            last = pe.matmul(ps_acc[:, t % 2, 0:TILE], table_parts[0:OH_P, part, t, c, :],
                                             one_hot[0:OH_P, t % 2, c, :], start=(c == 0 and part == 0),
                                             stop=(c == CHUNKS - 1 and part == PARTS - 1))
                    last.then_inc(look_done, 1)
                    if t + 2 < OH:
                        spread_ids(i, t + 2)

            def turn(i, u, b):
                for s in range(SUBS):
                    for g in range(GROUPS):
                        n = s * GROUPS + g
                        if n >= TURN_SLOTS:
                            pe.wait_ge(turn_out, TURNS * i + n + 1 - TURN_SLOTS)
                        elif n == 0 and not static(i, 0):
                            pe.wait_ge(gram_out_dve, 2 * GRAMS * i)
                            pe.wait_ge(gram_out_act, 2 * GRAMS * i)
                        pe.wait_ge(rows_in[b][s][g], 16 * GROUP * (u + 1))
                        for k in range(GROUP):
                            last = pe.transpose(ps_turn[:, n % TURN_SLOTS, k, :], rows[:, b, s, g * GROUP + k, :], ident[:, :])
                        last.then_inc(turned[b], 1)

            def grams(i):
                pe.wait_ge(x_out, i + 1)
                pe.wait_ge(look_out, OH * (i + 1))
                pe.wait_ge(turn_out, TURNS * (i + 1))
                for g in range(GRAMS):
                    if g >= 2:
                        pe.wait_ge(gram_out_dve, 2 * (GRAMS * i + g - 1))
                        pe.wait_ge(gram_out_act, 2 * (GRAMS * i + g - 1))
                    for q in range(PER):
                        quad = ET[:, g * PER + q, :, :]
                        last = pe.matmul(ps_gram[:, g % 2, q, 0:QUAD * COLS], quad, quad[:, :, 1:FEATURES],
                                         start=True, stop=True)
                    last.then_inc(gram_done, 1)

            def mlp(i, b, after_look):
                for m in range(L1_BLOCKS):
                    if m >= 2:
                        pe.wait_ge(acc_out, MLP_USES * i + m - 1)
                    elif after_look:
                        pe.wait_ge(look_out, OH * (i + 2))
                    else:
                        pe.wait_ge(acc_out, MLP_USES * i)
                    w = slice(m * P, (m + 1) * P)
                    pe.matmul(ps_acc[:, m % 2, 0:TILE], w1_sb[:, PAIR_CHUNKS, w], x_sb[:, bass.ds(i * TILE, TILE)],
                              start=True, stop=False)
                    if m == 0:
                        pe.wait_ge(z_in, 16 * len(MOVES) * (i + 1))
                    for c in range(PAIR_CHUNKS):
                        k = min(P, PAIRS - c * P)
                        last = pe.matmul(ps_acc[:, m % 2, 0:TILE], w1_sb[0:k, c, w], z[b][0:k, c, :],
                                         start=False, stop=(c == PAIR_CHUNKS - 1))
                    last.then_inc(acc_done, 1)
                for m in range(L2_BLOCKS):
                    n = L1_BLOCKS + m
                    pe.wait_ge(acc_out, MLP_USES * i + (L1_BLOCKS if m == 0 else n - 1))
                    for c in range(L1_BLOCKS):
                        last = pe.matmul(ps_acc[:, n % 2, 0:TILE], w2_sb[:, c, m * P:(m + 1) * P], h1[:, c, :],
                                         start=(c == 0), stop=(c == L1_BLOCKS - 1))
                        if m == 0 and c == 0:
                            last.then_inc(z_read[b], 1)
                    last.then_inc(acc_done, 1)
                n = MLP_USES - 1
                pe.wait_ge(acc_out, MLP_USES * i + n)
                for c in range(L2_BLOCKS):
                    last = pe.matmul(ps_acc[0:1, n % 2, 0:TILE], w3_sb[:, c:c + 1], h2[:, c, :],
                                     start=(c == 0), stop=(c == L2_BLOCKS - 1))
                last.then_inc(acc_done, 1)

            def tile(i, u, b):
                look_up(i)
                turn(i, u, b)
                grams(i)
                if not static(i, 0):
                    mlp(i - 1, 1 - b, True)

            pe.wait_ge(consts, 4)
            pe.wait_ge(ids_cast, 1)
            pe.wait_ge(x_in, 16)
            pe.wait_ge(w_in, 16 * WEIGHT_LOADS)
            pe.wait_ge(part_lo, OH)
            pe.wait_ge(w1_summed, 1)
            for b in range(2):
                tile(b, 0, b)
            with pe.Fori(1, TILES // 2) as u:
                for b in range(2):
                    tile(2 * u + b, u, b)
            mlp(TILES - 1, 1, False)


def kernel(**inputs):
    import concourse.bacc as bacc
    from concourse.bass_utils import run_bass_kernel_spmd

    nc = bacc.Bacc("TRN2", target_bir_lowering=False, num_devices=1)
    arrays = {}

    def given(name, array):
        arrays[name] = np.ascontiguousarray(array)
        return nc.dram_tensor(name, arrays[name].shape, mybir.dt.from_np(arrays[name].dtype), kind="ExternalInput").ap()

    ids = np.asarray(inputs["ids"])
    x_t = given("x_t", np.asarray(inputs["r_dense_features"]).T)
    ids_gather = given("ids_gather", ids[:, GATHERED])
    ids_one_hot = given("ids_one_hot", ids[:, ONE_HOT].T)
    tables = [given(f"tbl_{f}", np.asarray(inputs[f"tbl_{f}"])) for f in range(FIELDS)]
    w1 = given("w1", np.asarray(inputs["W_top1"])[weight_rows()])
    b1 = given("b1", np.asarray(inputs["b_top1"]).reshape(L1_BLOCKS, P).T)
    w2 = given("w2", np.asarray(inputs["W_top2"]))
    b2 = given("b2", np.asarray(inputs["b_top2"]).reshape(L2_BLOCKS, P).T)
    w3 = given("w3", np.asarray(inputs["W_top3"]).reshape(L2_BLOCKS, P).T)
    out = nc.dram_tensor("out", (BATCH, 1), F32, kind="ExternalOutput").ap()
    build(nc, x_t, ids_gather, ids_one_hot, tables, w1, b1, w2, b2, w3, out)
    r = run_bass_kernel_spmd(nc, [arrays], core_ids=[0])
    return r.results[0]["out"]
```

```python
from contextlib import ExitStack

import numpy as np

import concourse.bass as bass
from concourse import mybir

P = 128
BATCH = 2048
D = 128
FIELDS = 26
FEATURES = FIELDS + 1
TILE = 256
TILES = BATCH // TILE
SUBS = TILE // P
H1, H2 = 512, 256

ONE_HOT = [0, 4, 8, 10, 12, 16, 17]
GATHERED = [f for f in range(FIELDS) if f not in ONE_HOT]
OH = len(ONE_HOT)
OH_ROWS = 1000
CHUNKS = 8
OH_P = OH_ROWS // CHUNKS
HALF = CHUNKS // 2

GATHERS = len(GATHERED)
WEIGHT_LOADS = 9
GROUP = 4
GROUPS = -(-GATHERS // GROUP)
FIRST_GROUP = GATHERS - (GROUPS - 1) * GROUP
TURN_SLOTS = 4
AHEAD = 2
BANK = 512

FPAD = 32
QUAD = 4
COLS = FEATURES - 1
QUADS = P // QUAD
PER = 8
GRAMS = QUADS // PER

ORDER = [0] + [1 + f for f in ONE_HOT] + [1 + f for f in GATHERED]
PAIRS = FEATURES * COLS // 2

STRIPS = [(i, 4, i + 4, FEATURES - i - 4) for i in range(0, FEATURES - 4, 4)]
CORNERS = [(i, min(3, FEATURES - 1 - i), i + 1, min(3, FEATURES - 1 - i)) for i in range(0, FEATURES - 1, 4)]
RECTS = [[STRIPS[0], STRIPS[4], CORNERS[6]], [STRIPS[1], STRIPS[3]], [STRIPS[2], STRIPS[5]] + CORNERS[:6]]
PAIR_CHUNKS = len(RECTS)
CHUNK_ROWS = [sum(n * m for _, n, _, m in rects) for rects in RECTS]
assert max(CHUNK_ROWS) <= P


def pair_start(i):
    return i * COLS - i * (i - 1) // 2


def lay_out_w1(w):
    chunks = []
    for rects in RECTS:
        chunk, at = np.zeros((P, w.shape[1]), w.dtype), 0
        for i0, n, j0, m in rects:
            for i in range(i0, i0 + n):
                for j in range(j0, j0 + m):
                    if i < j:
                        a, b = sorted((ORDER[i], ORDER[j]))
                        chunk[at] = w[D + pair_start(a) + b - a - 1]
                    at += 1
        chunks.append(chunk)
    return np.stack(chunks + [w[:D], w[D + PAIRS:]])


MOVES = sum(len(rects) for rects in RECTS)

F32 = mybir.dt.float32
F32R = mybir.dt.float32r
F16 = mybir.dt.float16
I32 = mybir.dt.int32
ALU = mybir.AluOpType
ACT = mybir.ActivationFunctionType

L1_BLOCKS = H1 // P
L2_BLOCKS = H2 // P
MLP_USES = L1_BLOCKS + L2_BLOCKS + 1


def build(nc, x_t, ids_gather, ids_one_hot, tables, w1, b1, w2, b2, w3, out):
    with ExitStack() as ctx:
        def sb(name, shape, dt=F32):
            return ctx.enter_context(nc.sbuf_tensor(name, shape, dt))

        def psum(name, shape):
            return ctx.enter_context(nc.psum_tensor(name, shape, F32))

        def sem(name):
            return ctx.enter_context(nc.semaphore(name))

        ident = sb("ident", [P, P])
        select = sb("select", [P, OH, P], F16)
        row_i = sb("row_i", [P, CHUNKS], I32)
        row_f = sb("row_f", [P, CHUNKS])
        table_parts = sb("table_parts", [P, 2, OH, CHUNKS, D], F32R)
        idx = [sb(f"idx{s}", [P, GATHERS], I32) for s in range(SUBS)]
        oh_ids_h = sb("oh_ids_h", [P, BATCH], F16)
        one_hot = sb("one_hot", [P, 2, CHUNKS, TILE], F32R)
        x_sb = sb("x_sb", [P, BATCH])
        rows = sb("rows", [P, SUBS, GATHERS, D])
        ET = sb("ET", [P, SUBS, QUADS, QUAD, FPAD])
        gram = sb("gram", [P, COLS, TILE])
        z = sb("z", [P, PAIR_CHUNKS, TILE])
        w1_sb = sb("w1_sb", [P, PAIR_CHUNKS + 1, H1])
        w2_sb = sb("w2_sb", [P, L1_BLOCKS, H2])
        w3_sb = sb("w3_sb", [P, L2_BLOCKS])
        b1_sb = sb("b1_sb", [P, L1_BLOCKS])
        b2_sb = sb("b2_sb", [P, L2_BLOCKS])
        h1 = sb("h1", [P, L1_BLOCKS, TILE])
        h2 = sb("h2", [P, L2_BLOCKS, TILE])
        y = sb("y", [1, BATCH])
        table_f32 = ET[:, :, :, :, :].rearrange("p s q r f -> p (s q r f)")[:, 0:OH * CHUNKS * D]
        oh_ids = gram[0:OH, 0:BATCH // TILE, :].rearrange("t j b -> t (j b)").bitcast(I32)
        w1_again = gram[:, COLS - H1 // TILE:COLS, :].rearrange("p j b -> p (j b)")
        table_f32 = table_f32.rearrange("p (t c d) -> p t c d", t=OH, c=CHUNKS)

        ps_blocks = psum("ps_blocks", [P, TURN_SLOTS * GROUP, P])
        ps_turn = ps_blocks[:, :, :].rearrange("p (slot k) b -> p slot k b", k=GROUP)
        ps_gram = ps_blocks[:, :, :].rearrange("p (slot q) c -> p slot q c", q=PER)
        ps_ids = psum("ps_ids", [P, 2, BANK])
        ps_acc = psum("ps_acc", [P, 2, BANK])

        idx_in = [sem(f"idx_in{s}") for s in range(SUBS)]
        oh_ids_in = sem("oh_ids_in")
        x_in = sem("x_in")
        rows_in = [[sem(f"rows_in{s}_{g}") for g in range(GROUPS)] for s in range(SUBS)]
        w_in = sem("w_in")
        table_in = [sem(f"table_in{t}") for t in range(OH)]
        zeroed = sem("zeroed")
        consts = sem("consts")
        row_f_done = sem("row_f_done")
        ids_zero = sem("ids_zero")
        ids_cast = sem("ids_cast")
        part_hi = sem("part_hi")
        part_lo = sem("part_lo")
        pad_zero = sem("pad_zero")
        w1_summed = sem("w1_summed")
        ids_spread = sem("ids_spread")
        one_hot_done = sem("one_hot_done")
        half_done = sem("half_done")
        look_out = sem("look_out")
        turned = [sem(f"turned{s}") for s in range(SUBS)]
        turn_out = sem("turn_out")
        x_out = sem("x_out")
        gram_done = sem("gram_done")
        gram_out_dve = sem("gram_out_dve")
        gram_out_act = sem("gram_out_act")
        z_in = sem("z_in")
        acc_done = sem("acc_done")
        acc_out = sem("acc_out")
        z_read = sem("z_read")
        y_out = sem("y_out")

        def static(i, *tiles):
            return isinstance(i, int) and i in tiles

        def group(g):
            return (FIRST_GROUP, 0) if g == 0 else (GROUP, FIRST_GROUP + (g - 1) * GROUP)

        def gram_block(s, g, r):
            at = s * P + r * QUADS + g * PER
            return (gram[0:COLS, :, at:at + PER],
                    ps_gram[r * FPAD:r * FPAD + COLS, g % 2, :, r * COLS:(r + 1) * COLS].rearrange("i q j -> i j q"))

        def by_sample(features):
            return features.rearrange("d s q r -> d s r q")

        def in_samples(source):
            return source.rearrange("d (s r q) -> d s r q", s=SUBS, r=QUAD)

        block = ctx.enter_context(nc.Block())

        @block.sync
        def _(sp):
            def load_idx(first, s):
                sp.dma_start(idx[s][:, :], ids_gather[bass.ds(first, P), :]).then_inc(idx_in[s], 16)

            def next_idx(i, s):
                first = sp.snap((i + 1) * TILE + s * P)
                sp.wait_ge(turned[s], GROUPS * (i + 1))
                load_idx(first, s)

            def move_pairs(i):
                copies = sp.snap(2 * SUBS * GRAMS * (i + 1))
                sp.wait_ge(gram_out_act, copies)
                sp.wait_ge(gram_out_dve, copies)
                if not static(i, 0):
                    sp.wait_ge(z_read, i)
                for c, rects in enumerate(RECTS):
                    p = 0
                    for i0, n, j0, m in rects:
                        sp.dma_start(z[p:p + n * m, c, :], gram[i0:i0 + n, j0 - 1:j0 - 1 + m, :]).then_inc(z_in, 16)
                        p += n * m

            for s in range(SUBS):
                load_idx(s * P, s)
            sp.dma_start(oh_ids[:, :], ids_one_hot).then_inc(oh_ids_in, 16)
            for t in range(OH):
                sp.dma_start(table_f32[0:OH_P, t, :, :], tables[ONE_HOT[t]].rearrange(
                    "(p c) d -> p c d", c=CHUNKS)).then_inc(table_in[t], 16)
            sp.dma_start(x_sb[:, :], x_t).then_inc(x_in, 16)
            for c in range(PAIR_CHUNKS + 1):
                sp.dma_start(w1_sb[:, c, :], w1[c, :, :]).then_inc(w_in, 16)
            sp.dma_start(w1_again, w1[PAIR_CHUNKS + 1, :, :]).then_inc(w_in, 16)
            sp.dma_start(w2_sb[:, :, :], w2.rearrange("(c p) n -> p c n", p=P)).then_inc(w_in, 16)
            sp.dma_start(w3_sb[:, :], w3).then_inc(w_in, 16)
            sp.dma_start(b1_sb[:, :], b1).then_inc(w_in, 16)
            sp.dma_start(b2_sb[:, :], b2).then_inc(w_in, 16)

            def tile(i, more=True):
                if more:
                    for s in range(SUBS):
                        next_idx(i, s)
                move_pairs(i)

            tile(0)
            with sp.Fori(1, TILES - 1) as i:
                tile(i)
            tile(TILES - 1, more=False)

        @block.gpsimd
        def _(pool):
            pool.memset(ident[:, :], 0.0).then_inc(zeroed, 1)
            pool.memset(select[:, :, :], 0.0).then_inc(zeroed, 1)
            pool.iota(row_i[:, :], pattern=[[1, CHUNKS]], base=0, channel_multiplier=CHUNKS).then_inc(consts, 1)
            pool.wait_ge(zeroed, 2)
            pool.affine_select(out=ident[:, :], in_=ident[:, :], compare_op=ALU.not_equal, fill=1.0, base=0,
                               pattern=[[-1, P]], channel_multiplier=1).then_inc(consts, 1)
            pool.affine_select(out=select[:, :, :], in_=select[:, :, :], compare_op=ALU.not_equal, fill=1.0,
                               base=0, pattern=[[-1, OH], [0, P]], channel_multiplier=1).then_inc(consts, 1)

            def gather(s):
                for n, f in enumerate(GATHERED):
                    pool.indirect_dma_start(
                        out=rows[:, s, n, :], out_offset=None, in_=tables[f],
                        in_offset=bass.IndirectOffsetOnAxis(ap=idx[s][:, n:n + 1], axis=0),
                    ).then_inc(rows_in[s][(n + GROUP - FIRST_GROUP) // GROUP], 16)

            for s in range(SUBS):
                pool.wait_ge(idx_in[s], 16)
                gather(s)
            landed = [pool.alloc_register(f"landed{s}") for s in range(SUBS)]
            for s in range(SUBS):
                pool.reg_mov(landed[s], 32)
            with pool.Fori(1, TILES) as i:
                for s in range(SUBS):
                    count = pool.snap(landed[s])
                    pool.wait_ge(turned[s], GROUPS * i)
                    pool.wait_ge(idx_in[s], count)
                    pool.reg_add(landed[s], landed[s], 16)
                    gather(s)

        @block.vector
        def _(dve):
            dve.memset(oh_ids_h[:, :], 0.0).then_inc(ids_zero, 1)
            dve.wait_ge(consts, 3)
            dve.tensor_copy(row_f[:, :], row_i[:, :]).then_inc(row_f_done, 1)
            dve.wait_ge(oh_ids_in, 16)
            dve.wait_ge(ids_zero, 1)
            dve.tensor_copy(oh_ids_h[0:OH, :], oh_ids[:, :]).then_inc(ids_cast, 1)
            for t in range(OH):
                dve.wait_ge(part_hi, t + 1)
                dve.tensor_tensor(table_parts[0:OH_P, 1, t, :, :], table_f32[0:OH_P, t, :, :],
                                  table_parts[0:OH_P, 0, t, :, :], ALU.subtract).then_inc(part_lo, 1)
            dve.wait_ge(part_lo, OH)
            dve.memset(ET[:, :, :, :, FEATURES:FPAD], 0.0).then_inc(pad_zero, 1)
            dve.wait_ge(w_in, 16 * WEIGHT_LOADS)
            dve.tensor_tensor(w1_sb[:, PAIR_CHUNKS, :], w1_sb[:, PAIR_CHUNKS, :], w1_again[:, :],
                              ALU.add).then_inc(w1_summed, 1)
            dve.wait_ge(row_f_done, 1)

            def one_hots(i, ts):
                for t in ts:
                    dve.wait_ge(ids_spread, OH * i + t + 1)
                    for h in range(2):
                        if t >= 2:
                            dve.wait_ge(half_done, 2 * (OH * i + t - 2) + h + 1)
                        elif not static(i, 0) and t == 0 and h == 0:
                            dve.wait_ge(half_done, 2 * OH * i)
                        dve.tensor_tensor(
                            one_hot[0:OH_P, t % 2, h * HALF:(h + 1) * HALF, :],
                            ps_ids[0:OH_P, t % 2, 0:TILE].unsqueeze(1).to_broadcast([OH_P, HALF, TILE]),
                            row_f[0:OH_P, h * HALF:(h + 1) * HALF].unsqueeze(2).to_broadcast([OH_P, HALF, TILE]),
                            ALU.is_equal).then_inc(one_hot_done, 1)

            def gram_out(i, s):
                if s == 0 and not static(i, 0):
                    dve.wait_ge(z_in, 16 * MOVES * i)
                for g in range(GRAMS):
                    dve.wait_ge(gram_done, GRAMS * (SUBS * i + s) + g + 1)
                    for r in (0, 1):
                        dve.tensor_copy(*gram_block(s, g, r)).then_inc(gram_out_dve, 1)

            def tile(i, more=True):
                one_hots(i, range(AHEAD, OH))
                gram_out(i, 0)
                if more:
                    one_hots(i + 1, range(AHEAD))
                gram_out(i, 1)

            one_hots(0, range(AHEAD))
            tile(0)
            with dve.Fori(1, TILES - 1) as i:
                tile(i)
            tile(TILES - 1, more=False)

        @block.scalar
        def _(act):
            for t in range(OH):
                act.wait_ge(table_in[t], 16)
                act.activation(table_parts[0:OH_P, 0, t, :, :], table_f32[0:OH_P, t, :, :], ACT.Copy).then_inc(part_hi, 1)
            act.wait_ge(x_in, 16)
            act.wait_ge(w_in, 16 * WEIGHT_LOADS)
            act.wait_ge(part_lo, OH)

            def features(i):
                if not static(i, 0):
                    act.wait_ge(gram_done, SUBS * GRAMS * i)
                act.activation(by_sample(ET[:, :, :, :, 0]), in_samples(x_sb[:, bass.ds(i * TILE, TILE)]),
                               ACT.Copy).then_inc(x_out, 1)
                for t in range(OH):
                    act.wait_ge(half_done, 2 * (OH * i + t + 1))
                    act.activation(by_sample(ET[:, :, :, :, 1 + t]), in_samples(ps_acc[:, t % 2, 0:TILE]),
                                   ACT.Copy).then_inc(look_out, 1)

            def copy_turned(i, s):
                for g in range(GROUPS):
                    act.wait_ge(turned[s], GROUPS * i + g + 1)
                    k, f = group(g)
                    f += 1 + OH
                    act.activation(ET[:, s, :, :, f:f + k].rearrange("d q r f -> d f r q"),
                                   ps_turn[:, g % TURN_SLOTS, 0:k, :].rearrange("d f (r q) -> d f r q", q=QUADS),
                                   ACT.Copy).then_inc(turn_out, 1)

            def gram_out(i, s):
                if s == 0 and not static(i, 0):
                    act.wait_ge(z_in, 16 * MOVES * i)
                for g in range(GRAMS):
                    act.wait_ge(gram_done, GRAMS * (SUBS * i + s) + g + 1)
                    for r in (2, 3):
                        act.activation(*gram_block(s, g, r), ACT.Copy).then_inc(gram_out_act, 1)

            def relu(i, n, out, bias):
                act.wait_ge(acc_done, MLP_USES * i + n + 1)
                act.activation(out, ps_acc[:, n % 2, 0:TILE], ACT.Relu, bias=bias).then_inc(acc_out, 1)

            def layer_1_out(i):
                for m in range(L1_BLOCKS):
                    relu(i, m, h1[:, m, :], b1_sb[:, m:m + 1])

            def layer_2_out(i):
                for m in range(L2_BLOCKS):
                    relu(i, L1_BLOCKS + m, h2[:, m, :], b2_sb[:, m:m + 1])

            def layer_3_out(i):
                act.wait_ge(acc_done, MLP_USES * (i + 1))
                act.activation(y[:, bass.ds(i * TILE, TILE)], ps_acc[0:1, (MLP_USES - 1) % 2, 0:TILE],
                               ACT.Copy).then_inc(acc_out, 1)

            def tile(i, last=False):
                features(i)
                copy_turned(i, 0)
                gram_out(i, 0)
                if not static(i, 0) and not last:
                    layer_1_out(i - 1)
                copy_turned(i, 1)
                if not static(i, 0) and not last:
                    layer_2_out(i - 1)
                gram_out(i, 1)
                if not static(i, 0) and not last:
                    layer_3_out(i - 1)

            tile(0)
            with act.Fori(1, TILES - 1) as i:
                tile(i)
            tile(TILES - 1, last=True)
            for i in (TILES - 2, TILES - 1):
                layer_1_out(i)
                layer_2_out(i)
                layer_3_out(i)
            act.wait_ge(acc_out, MLP_USES * TILES)
            act.dma_start(out.rearrange("b o -> o b"), y[:, :]).then_inc(y_out, 16)
            act.wait_ge(y_out, 16)

        @block.tensor
        def _(pe):
            def spread_ids(i, t):
                pe.matmul(ps_ids[0:OH_P, t % 2, 0:TILE], select[:, t, 0:OH_P], oh_ids_h[:, bass.ds(i * TILE, TILE)],
                          start=True, stop=True).then_inc(ids_spread, 1)

            def spread_ahead(i):
                if not static(i, 0):
                    pe.wait_ge(one_hot_done, 2 * OH * i)
                for t in range(2):
                    spread_ids(i, t)

            def look_up(i):
                for t in range(OH):
                    if t >= 2:
                        pe.wait_ge(look_out, OH * i + t - 1)
                    elif static(i, 1):
                        pe.wait_ge(look_out, OH)
                    elif not static(i, 0):
                        pe.wait_ge(acc_out, MLP_USES * (i - 1))
                    for h in range(2):
                        pe.wait_ge(one_hot_done, 2 * (OH * i + t) + h + 1)
                        for c in range(HALF):
                            for part in range(2):
                                last = pe.matmul(ps_acc[:, t % 2, 0:TILE], table_parts[0:OH_P, part, t, h * HALF + c, :],
                                                 one_hot[0:OH_P, t % 2, h * HALF + c, :], start=(h + c + part == 0),
                                                 stop=(h == 1 and c == HALF - 1 and part == 1))
                        last.then_inc(half_done, 1)
                    if t + 2 < OH:
                        spread_ids(i, t + 2)

            def turn(i, s):
                for g in range(GROUPS):
                    if g >= TURN_SLOTS:
                        pe.wait_ge(turn_out, GROUPS * (SUBS * i + s) + g + 1 - TURN_SLOTS)
                    elif g == 0 and not (static(i, 0) and s == 0):
                        pe.wait_ge(gram_out_dve, 2 * GRAMS * (SUBS * i + s))
                        pe.wait_ge(gram_out_act, 2 * GRAMS * (SUBS * i + s))
                    count, f = group(g)
                    pe.wait_ge(rows_in[s][g], 16 * count * (i + 1))
                    for k in range(count):
                        last = pe.transpose(ps_turn[:, g % TURN_SLOTS, k, :], rows[:, s, f + k, :], ident[:, :])
                    last.then_inc(turned[s], 1)

            def grams(i, s):
                if s == 0:
                    pe.wait_ge(x_out, i + 1)
                    pe.wait_ge(look_out, OH * (i + 1))
                pe.wait_ge(turn_out, GROUPS * (SUBS * i + s + 1))
                for g in range(GRAMS):
                    if g >= 2:
                        pe.wait_ge(gram_out_dve, 2 * (GRAMS * (SUBS * i + s) + g - 1))
                        pe.wait_ge(gram_out_act, 2 * (GRAMS * (SUBS * i + s) + g - 1))
                    for q in range(PER):
                        quad = ET[:, s, g * PER + q, :, :]
                        last = pe.matmul(ps_gram[:, g % 2, q, 0:QUAD * COLS], quad, quad[:, :, 1:FEATURES],
                                         start=True, stop=True)
                    last.then_inc(gram_done, 1)

            def layer_1(i, after_look):
                for m in range(L1_BLOCKS):
                    if m >= 2:
                        pe.wait_ge(acc_out, MLP_USES * i + m - 1)
                    elif after_look:
                        pe.wait_ge(look_out, OH * (i + 2))
                    else:
                        pe.wait_ge(acc_out, MLP_USES * i)
                    w = slice(m * P, (m + 1) * P)
                    pe.matmul(ps_acc[:, m % 2, 0:TILE], w1_sb[:, PAIR_CHUNKS, w], x_sb[:, bass.ds(i * TILE, TILE)],
                              start=True, stop=False)
                    if m == 0:
                        pe.wait_ge(z_in, 16 * MOVES * (i + 1))
                    for c, k in enumerate(CHUNK_ROWS):
                        last = pe.matmul(ps_acc[:, m % 2, 0:TILE], w1_sb[0:k, c, w], z[0:k, c, :],
                                         start=False, stop=(c == PAIR_CHUNKS - 1))
                    last.then_inc(acc_done, 1)

            def layer_2(i):
                for m in range(L2_BLOCKS):
                    n = L1_BLOCKS + m
                    pe.wait_ge(acc_out, MLP_USES * i + L1_BLOCKS)
                    for c in range(L1_BLOCKS):
                        last = pe.matmul(ps_acc[:, n % 2, 0:TILE], w2_sb[:, c, m * P:(m + 1) * P], h1[:, c, :],
                                         start=(c == 0), stop=(c == L1_BLOCKS - 1))
                        if m == 0 and c == 0:
                            last.then_inc(z_read, 1)
                    last.then_inc(acc_done, 1)

            def layer_3(i):
                n = MLP_USES - 1
                pe.wait_ge(acc_out, MLP_USES * i + n)
                for c in range(L2_BLOCKS):
                    last = pe.matmul(ps_acc[0:1, n % 2, 0:TILE], w3_sb[:, c:c + 1], h2[:, c, :],
                                     start=(c == 0), stop=(c == L2_BLOCKS - 1))
                last.then_inc(acc_done, 1)

            def tile(i, last=False):
                look_up(i)
                turn(i, 0)
                grams(i, 0)
                if not last:
                    spread_ahead(i + 1)
                    if not static(i, 0):
                        layer_1(i - 1, after_look=True)
                turn(i, 1)
                if not static(i, 0) and not last:
                    layer_2(i - 1)
                grams(i, 1)
                if not static(i, 0) and not last:
                    layer_3(i - 1)

            pe.wait_ge(consts, 3)
            pe.wait_ge(ids_cast, 1)
            pe.wait_ge(x_in, 16)
            pe.wait_ge(w_in, 16 * WEIGHT_LOADS)
            pe.wait_ge(part_lo, OH)
            pe.wait_ge(pad_zero, 1)
            pe.wait_ge(w1_summed, 1)
            spread_ahead(0)
            tile(0)
            with pe.Fori(1, TILES - 1) as i:
                tile(i)
            tile(TILES - 1, last=True)
            for i in (TILES - 2, TILES - 1):
                layer_1(i, after_look=(i == TILES - 2))
                layer_2(i)
                layer_3(i)


def kernel(**inputs):
    import concourse.bacc as bacc
    from concourse.bass_utils import run_bass_kernel_spmd

    nc = bacc.Bacc("TRN2", target_bir_lowering=False, num_devices=1)
    arrays = {}

    def given(name, array):
        arrays[name] = np.ascontiguousarray(array)
        return nc.dram_tensor(name, arrays[name].shape, mybir.dt.from_np(arrays[name].dtype), kind="ExternalInput").ap()

    ids = np.asarray(inputs["ids"])
    x_t = given("x_t", np.asarray(inputs["r_dense_features"]).T)
    ids_gather = given("ids_gather", ids[:, GATHERED])
    ids_one_hot = given("ids_one_hot", ids[:, ONE_HOT].T)
    tables = [given(f"tbl_{f}", np.asarray(inputs[f"tbl_{f}"])) for f in range(FIELDS)]
    w1 = given("w1", lay_out_w1(np.asarray(inputs["W_top1"])))
    b1 = given("b1", np.asarray(inputs["b_top1"]).reshape(L1_BLOCKS, P).T)
    w2 = given("w2", np.asarray(inputs["W_top2"]))
    b2 = given("b2", np.asarray(inputs["b_top2"]).reshape(L2_BLOCKS, P).T)
    w3 = given("w3", np.asarray(inputs["W_top3"]).reshape(L2_BLOCKS, P).T)
    out = nc.dram_tensor("out", (BATCH, 1), F32, kind="ExternalOutput").ap()
    build(nc, x_t, ids_gather, ids_one_hot, tables, w1, b1, w2, b2, w3, out)
    r = run_bass_kernel_spmd(nc, [arrays], core_ids=[0])
    return r.results[0]["out"]
```

```python
from contextlib import ExitStack

import numpy as np

import concourse.bass as bass
from concourse import mybir

P = 128
BATCH = 2048
D = 128
FIELDS = 26
FEATURES = FIELDS + 1
TILE = 256
TILES = BATCH // TILE
SUBS = TILE // P
H1, H2 = 512, 256

ONE_HOT = [0, 4, 8, 10, 12, 16, 17]
GATHERED = [f for f in range(FIELDS) if f not in ONE_HOT]
OH = len(ONE_HOT)
OH_ROWS = 1000
CHUNKS = 8
OH_P = OH_ROWS // CHUNKS
HALF = CHUNKS // 2

GATHERS = len(GATHERED)
WEIGHT_LOADS = 7
GROUP = 4
GROUPS = -(-GATHERS // GROUP)
FIRST_GROUP = GATHERS - (GROUPS - 1) * GROUP
TURN_SLOTS = 4
assert GROUPS <= OH - 1
AHEAD = 2
BANK = 512

FPAD = 32
QUAD = 4
COLS = FEATURES - 1
QUADS = P // QUAD
PER = 8
GRAMS = QUADS // PER

ORDER = [0] + [1 + f for f in ONE_HOT] + [1 + f for f in GATHERED]
PAIRS = FEATURES * COLS // 2

STRIPS = [(i, 4, i + 4, FEATURES - i - 4) for i in range(0, FEATURES - 4, 4)]
CORNERS = [(i, min(3, FEATURES - 1 - i), i + 1, min(3, FEATURES - 1 - i)) for i in range(0, FEATURES - 1, 4)]
RECTS = [[STRIPS[0], STRIPS[4], CORNERS[6]], [STRIPS[1], STRIPS[3]], [STRIPS[2], STRIPS[5]] + CORNERS[:6]]
PAIR_CHUNKS = len(RECTS)
CHUNK_ROWS = [sum(n * m for _, n, _, m in rects) for rects in RECTS]
Z_ROWS = max(CHUNK_ROWS)
assert Z_ROWS <= P and Z_ROWS == CHUNK_ROWS[-1]


def pair_start(i):
    return i * COLS - i * (i - 1) // 2


def lay_out_w1(w):
    chunks = []
    for rects in RECTS:
        chunk, at = np.zeros((P, w.shape[1]), w.dtype), 0
        for i0, n, j0, m in rects:
            for i in range(i0, i0 + n):
                for j in range(j0, j0 + m):
                    if i < j:
                        a, b = sorted((ORDER[i], ORDER[j]))
                        chunk[at] = w[D + pair_start(a) + b - a - 1]
                    at += 1
        chunks.append(chunk)
    return np.stack(chunks + [w[:D], w[D + PAIRS:]])


MOVES = sum(len(rects) for rects in RECTS)
LAST_BY_POOL = 4

F32 = mybir.dt.float32
F32R = mybir.dt.float32r
F16 = mybir.dt.float16
I32 = mybir.dt.int32
ALU = mybir.AluOpType
ACT = mybir.ActivationFunctionType

L1_BLOCKS = H1 // P
L2_BLOCKS = H2 // P
PART_PRODUCTS = [(0, 0), (1, 0), (0, 1)]
MLP_USES = L1_BLOCKS + L2_BLOCKS + 1


def build(nc, x_t, ids_gather, ids_one_hot, tables, w1, b1, w2, b2, w3, out):
    with ExitStack() as ctx:
        def sb(name, shape, dt=F32):
            return ctx.enter_context(nc.sbuf_tensor(name, shape, dt))

        def psum(name, shape):
            return ctx.enter_context(nc.psum_tensor(name, shape, F32))

        def sem(name):
            return ctx.enter_context(nc.semaphore(name))

        ident = sb("ident", [P, P])
        select = sb("select", [P, OH, P], F16)
        row_i = sb("row_i", [P, CHUNKS], I32)
        row_f = sb("row_f", [P, CHUNKS])
        table_parts = sb("table_parts", [P, 2, OH, CHUNKS, D], F32R)
        idx = [sb(f"idx{s}", [P, GATHERS], I32) for s in range(SUBS)]
        oh_ids_h = sb("oh_ids_h", [P, BATCH], F16)
        one_hot = sb("one_hot", [P, 2, CHUNKS, TILE], F32R)
        x_sb = sb("x_sb", [P, BATCH])
        rows = sb("rows", [P, SUBS, GATHERS, D])
        ET = sb("ET", [P, SUBS, QUADS, QUAD, FPAD])
        gram = sb("gram", [P, COLS, TILE])
        z = sb("z", [P, PAIR_CHUNKS, TILE])
        z_parts = sb("z_parts", [P, 2, PAIR_CHUNKS, TILE], F32R)
        w1_dense = sb("w1_dense", [P, H1])
        w1_parts = sb("w1_parts", [P, 2, PAIR_CHUNKS, H1], F32R)
        w2_parts = sb("w2_parts", [P, 2, L1_BLOCKS, H2], F32R)
        w3_sb = sb("w3_sb", [P, L2_BLOCKS])
        b1_sb = sb("b1_sb", [P, L1_BLOCKS])
        b2_sb = sb("b2_sb", [P, L2_BLOCKS])
        h1 = sb("h1", [P, L1_BLOCKS, TILE])
        h1_parts = sb("h1_parts", [P, 2, L1_BLOCKS, TILE], F32R)
        h2 = h1[:, 0:L2_BLOCKS, :]
        y = x_sb[0:1, :]
        table_f32 = ET[:, :, :, :, :].rearrange("p s q r f -> p (s q r f)")[:, 0:OH * CHUNKS * D]
        oh_ids = gram[0:OH, 0:BATCH // TILE, :].rearrange("t j b -> t (j b)").bitcast(I32)
        gram_room = gram[:, BATCH // TILE:BATCH // TILE + 3 * H1 // TILE, :].rearrange("p (n j) b -> p n (j b)", n=3)
        w1_again = gram_room[:, 2, :]
        table_f32 = table_f32.rearrange("p (t c d) -> p t c d", t=OH, c=CHUNKS)

        ps_blocks = psum("ps_blocks", [P, TURN_SLOTS * GROUP, P])
        ps_turn = ps_blocks[:, :, :].rearrange("p (slot k) b -> p slot k b", k=GROUP)
        ps_gram = ps_blocks[:, :, :].rearrange("p (slot q) c -> p slot q c", q=PER)
        ps_ids = psum("ps_ids", [P, 2, BANK])
        ps_acc = psum("ps_acc", [P, 2, BANK])

        idx_in = [sem(f"idx_in{s}") for s in range(SUBS)]
        oh_ids_in = sem("oh_ids_in")
        x_in = sem("x_in")
        rows_in = [[sem(f"rows_in{s}_{g}") for g in range(GROUPS)] for s in range(SUBS)]
        w_dense_in = sem("w_dense_in")
        w_in = sem("w_in")
        table_in = [sem(f"table_in{t}") for t in range(OH)]
        zeroed = sem("zeroed")
        consts = sem("consts")
        row_f_done = sem("row_f_done")
        ids_zero = sem("ids_zero")
        ids_cast = sem("ids_cast")
        part_hi = sem("part_hi")
        part_lo = sem("part_lo")
        pad_filled = sem("pad_filled")
        w1_summed = sem("w1_summed")
        ids_spread = sem("ids_spread")
        one_hot_done = sem("one_hot_done")
        half_done = sem("half_done")
        look_out = sem("look_out")
        turned = [sem(f"turned{s}") for s in range(SUBS)]
        turn_out = sem("turn_out")
        x_out = sem("x_out")
        gram_done = sem("gram_done")
        gram_out_dve = sem("gram_out_dve")
        gram_out_act = sem("gram_out_act")
        z_in = sem("z_in")
        z_last_in = [sem(f"z_last_in{c}") for c in range(PAIR_CHUNKS)]
        z_pool_in = sem("z_pool_in")
        z_hi = sem("z_hi")
        z_lo = sem("z_lo")
        w_hi = sem("w_hi")
        w_lo = sem("w_lo")
        h1_lo = sem("h1_lo")
        acc_done = sem("acc_done")
        acc_out = sem("acc_out")
        y_out = sem("y_out")

        def static(i, *tiles):
            return isinstance(i, int) and i in tiles

        def group(g):
            return (FIRST_GROUP, 0) if g == 0 else (GROUP, FIRST_GROUP + (g - 1) * GROUP)

        def gram_block(s, g, r):
            at = s * P + r * QUADS + g * PER
            return (gram[0:COLS, :, at:at + PER],
                    ps_gram[r * FPAD:r * FPAD + COLS, g % 2, :, r * COLS:(r + 1) * COLS].rearrange("i q j -> i j q"))

        def moves(first, count):
            pairs = []
            for c, rects in enumerate(RECTS):
                p = 0
                for i0, n, j0, m in rects:
                    pairs.append((c, z[p:p + n * m, c, first:first + count],
                                  gram[i0:i0 + n, j0 - 1:j0 - 1 + m, first:first + count]))
                    p += n * m
            return pairs

        def last_piece(n):
            if n == 0:
                return slice(0, Z_ROWS), slice(0, PAIR_CHUNKS), slice(0, P)
            return slice(0, CHUNK_ROWS[n - 1]), slice(n - 1, n), slice(P, TILE)

        def layer_1_bank(j, m):
            return ps_ids[:, m - 2, 0:TILE] if static(j, TILES - 1) and m >= 2 else ps_acc[:, acc_slot(m), 0:TILE]

        w1_rooms = [z[:, 0:H1 // TILE, :].rearrange("p c b -> p (c b)"), gram_room[:, 0, :], gram_room[:, 1, :]]
        weight_pieces = [(w1_rooms[c], w1_parts[:, :, c, :]) for c in (1, 2, 0)]
        weight_pieces.append((h1[:, :, :].rearrange("p c b -> p (c b)"),
                              w2_parts[:, :, :, :].rearrange("p part c n -> p part (c n)")))
        IN_GRAM = 2

        def acc_slot(n):
            return (n + OH) % 2

        def by_sample(features):
            return features.rearrange("d s q r -> d s r q")

        def in_samples(source):
            return source.rearrange("d (s r q) -> d s r q", s=SUBS, r=QUAD)

        block = ctx.enter_context(nc.Block())

        @block.sync
        def _(sp):
            def load_idx(first, s):
                sp.dma_start(idx[s][:, :], ids_gather[bass.ds(first, P), :]).then_inc(idx_in[s], 16)

            def next_idx(i, s):
                first = sp.snap((i + 1) * TILE + s * P)
                sp.wait_ge(turned[s], GROUPS * (i + 1))
                load_idx(first, s)

            def move_pairs(i):
                if static(i, 0):
                    sp.wait_ge(w_lo, IN_GRAM + 1)
                copies = sp.snap(2 * SUBS * GRAMS * (i + 1))
                sp.wait_ge(gram_out_act, copies)
                sp.wait_ge(gram_out_dve, copies)
                if not static(i, 0):
                    sp.wait_ge(z_lo, i)
                for _, to, source in moves(0, TILE):
                    sp.dma_start(to, source).then_inc(z_in, 16)

            def move_last_pairs():
                sp.wait_ge(z_lo, TILES - 1)
                for s in range(SUBS):
                    copies = 2 * GRAMS * (SUBS * (TILES - 1) + s + 1)
                    sp.wait_ge(gram_out_act, copies)
                    sp.wait_ge(gram_out_dve, copies)
                    if s == 0:
                        for _, to, source in moves(0, P):
                            sp.dma_start(to, source).then_inc(z_in, 16)
                    else:
                        for c, to, source in moves(P, P)[:-LAST_BY_POOL]:
                            sp.dma_start(to, source).then_inc(z_last_in[c], 16)

            for s in range(SUBS):
                load_idx(s * P, s)
            sp.dma_start(oh_ids[:, :], ids_one_hot).then_inc(oh_ids_in, 16)
            for t in range(OH):
                sp.dma_start(table_f32[0:OH_P, t, :, :], tables[ONE_HOT[t]].rearrange(
                    "(p c) d -> p c d", c=CHUNKS)).then_inc(table_in[t], 16)
            sp.dma_start(x_sb[:, :], x_t).then_inc(x_in, 16)
            sp.dma_start(w1_dense[:, :], w1[PAIR_CHUNKS, :, :]).then_inc(w_dense_in, 16)
            sp.dma_start(w1_again, w1[PAIR_CHUNKS + 1, :, :]).then_inc(w_dense_in, 16)
            for c in (1, 2, 0):
                sp.dma_start(w1_rooms[c], w1[c, :, :]).then_inc(w_in, 16)
            sp.dma_start(h1[:, :, :], w2.rearrange("(c p) n -> p c n", p=P)).then_inc(w_in, 16)
            sp.dma_start(w3_sb[:, :], w3).then_inc(w_in, 16)
            sp.dma_start(b1_sb[:, :], b1).then_inc(w_in, 16)
            sp.dma_start(b2_sb[:, :], b2).then_inc(w_in, 16)

            def tile(i):
                for s in range(SUBS):
                    next_idx(i, s)
                move_pairs(i)

            tile(0)
            with sp.Fori(1, TILES - 1) as i:
                tile(i)
            move_last_pairs()

        @block.gpsimd
        def _(pool):
            pool.memset(ident[:, :], 0.0).then_inc(zeroed, 1)
            pool.memset(select[:, :, :], 0.0).then_inc(zeroed, 1)
            pool.iota(row_i[:, :], pattern=[[1, CHUNKS]], base=0, channel_multiplier=CHUNKS).then_inc(consts, 1)
            pool.wait_ge(zeroed, 2)
            pool.affine_select(out=ident[:, :], in_=ident[:, :], compare_op=ALU.not_equal, fill=1.0, base=0,
                               pattern=[[-1, P]], channel_multiplier=1).then_inc(consts, 1)
            pool.affine_select(out=select[:, :, :], in_=select[:, :, :], compare_op=ALU.not_equal, fill=1.0,
                               base=0, pattern=[[-1, OH], [0, P]], channel_multiplier=1).then_inc(consts, 1)

            def gather(s):
                for n, f in enumerate(GATHERED):
                    pool.indirect_dma_start(
                        out=rows[:, s, n, :], out_offset=None, in_=tables[f],
                        in_offset=bass.IndirectOffsetOnAxis(ap=idx[s][:, n:n + 1], axis=0),
                    ).then_inc(rows_in[s][(n + GROUP - FIRST_GROUP) // GROUP], 16)

            for s in range(SUBS):
                pool.wait_ge(idx_in[s], 16)
                gather(s)
            landed = [pool.alloc_register(f"landed{s}") for s in range(SUBS)]
            for s in range(SUBS):
                pool.reg_mov(landed[s], 32)
            with pool.Fori(1, TILES) as i:
                for s in range(SUBS):
                    count = pool.snap(landed[s])
                    pool.wait_ge(turned[s], GROUPS * i)
                    pool.wait_ge(idx_in[s], count)
                    pool.reg_add(landed[s], landed[s], 16)
                    gather(s)

            pool.wait_ge(z_lo, TILES - 1)
            pool.wait_ge(gram_out_act, 2 * SUBS * GRAMS * TILES)
            pool.wait_ge(gram_out_dve, 2 * SUBS * GRAMS * TILES)
            for _, to, source in moves(P, P)[-LAST_BY_POOL:]:
                pool.dma_start(to, source).then_inc(z_pool_in, 16)

        @block.vector
        def _(dve):
            dve.memset(oh_ids_h[:, :], 0.0).then_inc(ids_zero, 1)
            dve.wait_ge(consts, 3)
            dve.tensor_copy(row_f[:, :], row_i[:, :]).then_inc(row_f_done, 1)
            dve.wait_ge(oh_ids_in, 16)
            dve.wait_ge(ids_zero, 1)
            for part in (slice(0, TILE), slice(TILE, BATCH)):
                dve.tensor_copy(oh_ids_h[0:OH, part], oh_ids[:, part]).then_inc(ids_cast, 1)
            dve.wait_ge(row_f_done, 1)

            def low_part(t):
                dve.wait_ge(part_hi, t + 1)
                dve.tensor_tensor(table_parts[0:OH_P, 1, t, :, :], table_f32[0:OH_P, t, :, :],
                                  table_parts[0:OH_P, 0, t, :, :], ALU.subtract).then_inc(part_lo, 1)

            def one_hots(i, ts):
                for t in ts:
                    dve.wait_ge(ids_spread, OH * i + t + 1)
                    for h in range(2):
                        if t >= 2:
                            dve.wait_ge(half_done, 2 * (OH * i + t - 2) + h + 1)
                        elif not static(i, 0) and t == 0 and h == 0:
                            dve.wait_ge(half_done, 2 * OH * i)
                        dve.tensor_tensor(
                            one_hot[0:OH_P, t % 2, h * HALF:(h + 1) * HALF, :],
                            ps_ids[0:OH_P, t % 2, 0:TILE].unsqueeze(1).to_broadcast([OH_P, HALF, TILE]),
                            row_f[0:OH_P, h * HALF:(h + 1) * HALF].unsqueeze(2).to_broadcast([OH_P, HALF, TILE]),
                            ALU.is_equal).then_inc(one_hot_done, 1)

            def gram_out(i, s):
                if s == 0 and not static(i, 0):
                    dve.wait_ge(z_in, 16 * MOVES * i)
                for g in range(GRAMS):
                    dve.wait_ge(gram_done, GRAMS * (SUBS * i + s) + g + 1)
                    for r in (0, 1):
                        dve.tensor_copy(*gram_block(s, g, r)).then_inc(gram_out_dve, 1)

            def cut_weights(pieces):
                for n in pieces:
                    weights, parts = weight_pieces[n]
                    dve.wait_ge(w_hi, n + 1)
                    dve.tensor_tensor(parts[:, 1, :], weights, parts[:, 0, :], ALU.subtract).then_inc(w_lo, 1)

            def cut_z(j):
                dve.wait_ge(z_hi, j + 1)
                dve.tensor_tensor(z_parts[0:Z_ROWS, 1, :, :], z[0:Z_ROWS, :, :], z_parts[0:Z_ROWS, 0, :, :],
                                  ALU.subtract).then_inc(z_lo, 1)

            def cut_last_z(n):
                p, c, b = last_piece(n)
                dve.wait_ge(z_hi, TILES + n)
                dve.tensor_tensor(z_parts[p, 1, c, b], z[p, c, b], z_parts[p, 0, c, b], ALU.subtract).then_inc(z_lo, 1)

            def cut_h1(j, ms=range(L1_BLOCKS)):
                for m in ms:
                    dve.wait_ge(acc_out, MLP_USES * j + m + 1)
                    dve.tensor_tensor(h1_parts[:, 1, m, :], h1[:, m, :], h1_parts[:, 0, m, :],
                                      ALU.subtract).then_inc(h1_lo, 1)

            def tile(i):
                one_hots(i, range(AHEAD, OH))
                if static(i, 0):
                    dve.wait_ge(w_dense_in, 32)
                    dve.tensor_tensor(w1_dense[:, :], w1_dense[:, :], w1_again, ALU.add).then_inc(w1_summed, 1)
                    cut_weights(range(IN_GRAM))
                    dve.wait_ge(w1_summed, 1)
                    dve.wait_ge(w_lo, IN_GRAM)
                else:
                    cut_z(i - 1)
                gram_out(i, 0)
                if not static(i, 0):
                    cut_h1(i - 1)
                one_hots(i + 1, range(AHEAD))
                gram_out(i, 1)
                if static(i, 0):
                    cut_weights(range(IN_GRAM, len(weight_pieces)))

            for t in range(OH):
                if t < AHEAD:
                    one_hots(0, [t])
                low_part(t)
            tile(0)
            with dve.Fori(1, TILES - 1) as i:
                tile(i)
            one_hots(TILES - 1, range(AHEAD, OH))
            cut_z(TILES - 2)
            gram_out(TILES - 1, 0)
            cut_h1(TILES - 2, [0, 1])
            gram_out(TILES - 1, 1)
            cut_h1(TILES - 2, [2, 3])
            for n in range(1 + PAIR_CHUNKS):
                cut_last_z(n)
            cut_h1(TILES - 1)

        @block.scalar
        def _(act):
            for t in range(OH):
                act.wait_ge(table_in[t], 16)
                act.activation(table_parts[0:OH_P, 0, t, :, :], table_f32[0:OH_P, t, :, :], ACT.Copy).then_inc(part_hi, 1)
            act.wait_ge(x_in, 16)
            act.wait_ge(part_lo, OH)
            act.activation(ET[:, :, :, :, FEATURES:FPAD].rearrange("d s q r f -> d (s q r) f"),
                           ident[:, 0:1].unsqueeze(2).to_broadcast([P, SUBS * P, FPAD - FEATURES]),
                           ACT.Copy).then_inc(pad_filled, 1)

            def dense_out(i):
                if not static(i, 0):
                    act.wait_ge(gram_done, SUBS * GRAMS * i)
                act.activation(by_sample(ET[:, :, :, :, 0]), in_samples(x_sb[:, bass.ds(i * TILE, TILE)]),
                               ACT.Copy).then_inc(x_out, 1)

            def looked_up_out(i, t):
                act.wait_ge(half_done, 2 * (OH * i + t + 1))
                act.activation(by_sample(ET[:, :, :, :, 1 + t]), in_samples(ps_acc[:, t % 2, 0:TILE]),
                               ACT.Copy).then_inc(look_out, 1)

            def turned_out(i, s, g):
                act.wait_ge(turned[s], GROUPS * i + g + 1)
                k, f = group(g)
                f += 1 + OH
                act.activation(ET[:, s, :, :, f:f + k].rearrange("d q r f -> d f r q"),
                               ps_turn[:, g % TURN_SLOTS, 0:k, :].rearrange("d f (r q) -> d f r q", q=QUADS),
                               ACT.Copy).then_inc(turn_out, 1)

            def gram_out(i, s, g):
                if s == 0 and g == 0 and not static(i, 0):
                    act.wait_ge(z_in, 16 * MOVES * i)
                act.wait_ge(gram_done, GRAMS * (SUBS * i + s) + g + 1)
                for r in (2, 3):
                    act.activation(*gram_block(s, g, r), ACT.Copy).then_inc(gram_out_act, 1)

            def cut_weights(n):
                weights, parts = weight_pieces[n]
                act.activation(parts[:, 0, :], weights, ACT.Copy).then_inc(w_hi, 1)

            def cut_z(j):
                act.wait_ge(z_in, 16 * MOVES * (j + 1))
                act.activation(z_parts[0:Z_ROWS, 0, :, :], z[0:Z_ROWS, :, :], ACT.Copy).then_inc(z_hi, 1)

            def cut_last_z(n):
                p, c, b = last_piece(n)
                if n == 0:
                    act.wait_ge(z_in, 16 * MOVES * TILES)
                else:
                    by_pool = LAST_BY_POOL if n == PAIR_CHUNKS else 0
                    act.wait_ge(z_last_in[n - 1], 16 * (len(RECTS[n - 1]) - by_pool))
                    if by_pool:
                        act.wait_ge(z_pool_in, 16 * by_pool)
                act.activation(z_parts[p, 0, c, b], z[p, c, b], ACT.Copy).then_inc(z_hi, 1)

            def layer_1_out(j, ms=range(L1_BLOCKS)):
                for m in ms:
                    act.wait_ge(acc_done, MLP_USES * j + m + 1)
                    bias = b1_sb[:, m:m + 1]
                    act.activation(h1[:, m, :], layer_1_bank(j, m), ACT.Relu, bias=bias)
                    act.activation(h1_parts[:, 0, m, :], layer_1_bank(j, m), ACT.Relu, bias=bias).then_inc(acc_out, 1)

            def layer_2_out(j):
                for m in range(L2_BLOCKS):
                    act.wait_ge(acc_done, MLP_USES * j + L1_BLOCKS + m + 1)
                    act.activation(h2[:, m, :], ps_acc[:, acc_slot(L1_BLOCKS + m), 0:TILE], ACT.Relu,
                                   bias=b2_sb[:, m:m + 1]).then_inc(acc_out, 1)

            def layer_3_out(j):
                act.wait_ge(acc_done, MLP_USES * (j + 1))
                act.activation(y[:, bass.ds(j * TILE, TILE)], ps_acc[0:1, acc_slot(MLP_USES - 1), 0:TILE],
                               ACT.Copy).then_inc(acc_out, 1)

            def first_half(i):
                dense_out(i)
                for t in range(OH):
                    looked_up_out(i, t)
                    if 1 <= t <= GROUPS:
                        turned_out(i, 0, t - 1)
                    n = t - (OH - len(weight_pieces))
                    if static(i, 0) and n >= 0:
                        if n == 0:
                            act.wait_ge(w_in, 16 * WEIGHT_LOADS)
                        cut_weights(n)
                if static(i, 0):
                    act.wait_ge(w1_summed, 1)
                    act.wait_ge(w_lo, IN_GRAM)
                else:
                    act.wait_ge(w_lo, len(weight_pieces))
                    cut_z(i - 1)
                for g in range(GRAMS):
                    gram_out(i, 0, g)

            def tile(i):
                first_half(i)
                if not static(i, 0):
                    layer_1_out(i - 1)
                for g in range(GROUPS):
                    turned_out(i, 1, g)
                if not static(i, 0):
                    layer_2_out(i - 1)
                for g in range(GRAMS):
                    if g == GRAMS - 1 and not static(i, 0):
                        layer_3_out(i - 1)
                    gram_out(i, 1, g)

            tile(0)
            with act.Fori(1, TILES - 1) as i:
                tile(i)
            first_half(TILES - 1)
            layer_1_out(TILES - 2, [0])
            for g in range(GROUPS):
                turned_out(TILES - 1, 1, g)
            layer_1_out(TILES - 2, [1])
            for g in range(GRAMS):
                gram_out(TILES - 1, 1, g)
            layer_1_out(TILES - 2, [2, 3])
            cut_last_z(0)
            layer_2_out(TILES - 2)
            cut_last_z(1)
            layer_3_out(TILES - 2)
            for n in range(2, 1 + PAIR_CHUNKS):
                cut_last_z(n)
            layer_1_out(TILES - 1)
            layer_2_out(TILES - 1)
            layer_3_out(TILES - 1)
            act.wait_ge(acc_out, MLP_USES * TILES)
            act.dma_start(out.rearrange("b o -> o b"), y[:, :]).then_inc(y_out, 16)
            act.wait_ge(y_out, 16)

        @block.tensor
        def _(pe):
            def spread_ids(i, t):
                pe.matmul(ps_ids[0:OH_P, t % 2, 0:TILE], select[:, t, 0:OH_P], oh_ids_h[:, bass.ds(i * TILE, TILE)],
                          start=True, stop=True).then_inc(ids_spread, 1)

            def spread_ahead(i):
                if not static(i, 0):
                    pe.wait_ge(one_hot_done, 2 * OH * i)
                for t in range(2):
                    spread_ids(i, t)

            def look_up(i, t):
                if t >= 2:
                    pe.wait_ge(look_out, OH * i + t - 1)
                if static(i, 0):
                    pe.wait_ge(part_lo, t + 1)
                for h in range(2):
                    pe.wait_ge(one_hot_done, 2 * (OH * i + t) + h + 1)
                    for c in range(HALF):
                        for part in range(2):
                            last = pe.matmul(ps_acc[:, t % 2, 0:TILE], table_parts[0:OH_P, part, t, h * HALF + c, :],
                                             one_hot[0:OH_P, t % 2, h * HALF + c, :], start=(h + c + part == 0),
                                             stop=(h == 1 and c == HALF - 1 and part == 1))
                    last.then_inc(half_done, 1)
                if t + 2 < OH:
                    spread_ids(i, t + 2)

            def turn(i, s, g):
                if g >= TURN_SLOTS:
                    pe.wait_ge(turn_out, GROUPS * (SUBS * i + s) + g + 1 - TURN_SLOTS)
                elif g == 0 and not (static(i, 0) and s == 0):
                    pe.wait_ge(gram_out_dve, 2 * GRAMS * (SUBS * i + s))
                    pe.wait_ge(gram_out_act, 2 * GRAMS * (SUBS * i + s))
                count, f = group(g)
                pe.wait_ge(rows_in[s][g], 16 * count * (i + 1))
                for k in range(count):
                    last = pe.transpose(ps_turn[:, g % TURN_SLOTS, k, :], rows[:, s, f + k, :], ident[:, :])
                last.then_inc(turned[s], 1)

            def grams(i, s, g):
                if s == 0 and g == 0:
                    pe.wait_ge(x_out, i + 1)
                    pe.wait_ge(look_out, OH * (i + 1))
                if g == 0:
                    pe.wait_ge(turn_out, GROUPS * (SUBS * i + s + 1))
                elif g >= 2:
                    pe.wait_ge(gram_out_dve, 2 * (GRAMS * (SUBS * i + s) + g - 1))
                    pe.wait_ge(gram_out_act, 2 * (GRAMS * (SUBS * i + s) + g - 1))
                for q in range(PER):
                    quad = ET[:, s, g * PER + q, :, :]
                    last = pe.matmul(ps_gram[:, g % 2, q, 0:QUAD * COLS], quad, quad[:, :, 1:FEATURES],
                                     start=True, stop=True)
                last.then_inc(gram_done, 1)

            def layer_1_dense(j, m):
                if static(j, TILES - 1):
                    if m < 2:
                        pe.wait_ge(acc_out, MLP_USES * j - m)
                elif m >= 2:
                    pe.wait_ge(acc_out, MLP_USES * j + m - 1)
                else:
                    pe.wait_ge(look_out, OH * (j + 2) - 1 + m)
                pe.matmul(layer_1_bank(j, m), w1_dense[:, m * P:(m + 1) * P],
                          x_sb[:, bass.ds(j * TILE, TILE)], start=True, stop=False)

            def layer_1_chunk(j, m, c):
                k = CHUNK_ROWS[c]
                for w_part, z_part in PART_PRODUCTS:
                    last = pe.matmul(layer_1_bank(j, m), w1_parts[0:k, w_part, c, m * P:(m + 1) * P],
                                     z_parts[0:k, z_part, c, :], start=False,
                                     stop=(c == PAIR_CHUNKS - 1 and (w_part, z_part) == PART_PRODUCTS[-1]))
                return last

            def layer_1(j, ms=range(L1_BLOCKS)):
                for m in ms:
                    if m >= 2:
                        layer_1_dense(j, m)
                    if m == 0:
                        pe.wait_ge(z_lo, j + 1)
                    for c in range(PAIR_CHUNKS):
                        last = layer_1_chunk(j, m, c)
                    last.then_inc(acc_done, 1)

            def layer_2(j):
                if static(j, TILES - 1):
                    pe.wait_ge(acc_out, MLP_USES * j + 2)
                    order = [(m, c) for c in range(L1_BLOCKS) for m in range(L2_BLOCKS)]
                else:
                    pe.wait_ge(acc_out, MLP_USES * j + L1_BLOCKS - 1)
                    order = [(m, c) for m in range(L2_BLOCKS) for c in range(L1_BLOCKS)]
                for m, c in order:
                    if m == 0:
                        pe.wait_ge(h1_lo, L1_BLOCKS * j + c + 1)
                    for w_part, h_part in PART_PRODUCTS:
                        last = pe.matmul(ps_acc[:, acc_slot(L1_BLOCKS + m), 0:TILE],
                                         w2_parts[:, w_part, c, m * P:(m + 1) * P], h1_parts[:, h_part, c, :],
                                         start=(c == 0 and (w_part, h_part) == PART_PRODUCTS[0]),
                                         stop=(c == L1_BLOCKS - 1 and (w_part, h_part) == PART_PRODUCTS[-1]))
                    if c == L1_BLOCKS - 1:
                        last.then_inc(acc_done, 1)

            def layer_3(j):
                pe.wait_ge(acc_out, MLP_USES * (j + 1) - 1)
                for c in range(L2_BLOCKS):
                    last = pe.matmul(ps_acc[0:1, acc_slot(MLP_USES - 1), 0:TILE], w3_sb[:, c:c + 1], h2[:, c, :],
                                     start=(c == 0), stop=(c == L2_BLOCKS - 1))
                last.then_inc(acc_done, 1)

            def first_half(i):
                for t in range(OH):
                    look_up(i, t)
                    if 1 <= t <= GROUPS:
                        turn(i, 0, t - 1)
                if not static(i, TILES - 1):
                    spread_ahead(i + 1)
                if static(i, 0):
                    pe.wait_ge(pad_filled, 1)
                else:
                    pe.wait_ge(w_lo, len(weight_pieces))
                    for m in range(2):
                        layer_1_dense(i - 1, m)
                for g in range(GRAMS):
                    grams(i, 0, g)

            def tile(i):
                first_half(i)
                if not static(i, 0):
                    layer_1(i - 1)
                for g in range(GROUPS):
                    turn(i, 1, g)
                if not static(i, 0):
                    layer_2(i - 1)
                for g in range(GRAMS):
                    if g == GRAMS - 1 and not static(i, 0):
                        layer_3(i - 1)
                    grams(i, 1, g)
                if not static(i, 0):
                    pe.wait_ge(acc_out, MLP_USES * i)

            pe.wait_ge(consts, 3)
            pe.wait_ge(ids_cast, 1)
            spread_ahead(0)
            pe.wait_ge(ids_cast, 2)
            tile(0)
            pe.wait_ge(x_in, 16)
            pe.wait_ge(w1_summed, 1)
            pe.wait_ge(w_in, 16 * WEIGHT_LOADS)
            with pe.Fori(1, TILES - 1) as i:
                tile(i)
            last = TILES - 1
            first_half(last)
            layer_1(last - 1, [0])
            for g in range(GROUPS):
                turn(last, 1, g)
            layer_1(last - 1, [1])
            for g in range(GRAMS):
                grams(last, 1, g)
            layer_1(last - 1, [2, 3])
            layer_1_dense(last, 2)
            layer_2(last - 1)
            layer_1_dense(last, 3)
            layer_3(last - 1)
            layer_1_dense(last, 1)
            for c in range(PAIR_CHUNKS):
                pe.wait_ge(z_lo, TILES + c + 1)
                for m in ((1, 2, 3, 0) if c == 0 else range(L1_BLOCKS)):
                    if c == 0 and m == 0:
                        layer_1_dense(last, 0)
                    product = layer_1_chunk(last, m, c)
                    if c == PAIR_CHUNKS - 1:
                        product.then_inc(acc_done, 1)
            layer_2(last)
            layer_3(last)


def kernel(**inputs):
    import concourse.bacc as bacc
    from concourse.bass_utils import run_bass_kernel_spmd

    nc = bacc.Bacc("TRN2", target_bir_lowering=False, num_devices=1)
    arrays = {}

    def given(name, array):
        arrays[name] = np.ascontiguousarray(array)
        return nc.dram_tensor(name, arrays[name].shape, mybir.dt.from_np(arrays[name].dtype), kind="ExternalInput").ap()

    ids = np.asarray(inputs["ids"])
    x_t = given("x_t", np.asarray(inputs["r_dense_features"]).T)
    ids_gather = given("ids_gather", ids[:, GATHERED])
    ids_one_hot = given("ids_one_hot", ids[:, ONE_HOT].T)
    tables = [given(f"tbl_{f}", np.asarray(inputs[f"tbl_{f}"])) for f in range(FIELDS)]
    w1 = given("w1", lay_out_w1(np.asarray(inputs["W_top1"])))
    b1 = given("b1", np.asarray(inputs["b_top1"]).reshape(L1_BLOCKS, P).T)
    w2 = given("w2", np.asarray(inputs["W_top2"]))
    b2 = given("b2", np.asarray(inputs["b_top2"]).reshape(L2_BLOCKS, P).T)
    w3 = given("w3", np.asarray(inputs["W_top3"]).reshape(L2_BLOCKS, P).T)
    out = nc.dram_tensor("out", (BATCH, 1), F32, kind="ExternalOutput").ap()
    build(nc, x_t, ids_gather, ids_one_hot, tables, w1, b1, w2, b2, w3, out)
    r = run_bass_kernel_spmd(nc, [arrays], core_ids=[0])
    return r.results[0]["out"]
```
